# Optimizing a Trainium2 kernel written in Bass

```python
import numpy as np
import jax
import jax.numpy as jnp

def _softmax(x, axis=-1):
    return jax.nn.softmax(x, axis=axis)

def _gelu(x):
    return jax.nn.gelu(x, approximate=True)

def _silu(x):
    return jax.nn.silu(x)

def _sigmoid(x):
    return jax.nn.sigmoid(x)

def _layernorm(x, axis=-1, eps=1e-05):
    m = jnp.mean(x, axis=axis, keepdims=True)
    v = jnp.var(x, axis=axis, keepdims=True)
    return (x - m) / jnp.sqrt(v + eps)

def _scatter_add(tgt, idx, src, axis=0):
    return tgt.at[idx].add(src)

def _segment_sum(src, seg, n):
    return jax.ops.segment_sum(src, seg, n)
kernel_name = 'mk_dlrm_tower_d1_rec_r8_d6fb11'

def setup_inputs(seed: int=0):
    np.random.seed(seed)
    _w = jnp.asarray

    def _rec_inputs():
        import jax
        import jax.numpy as jnp
        _tk = jax.random.key(seed)
        ids = jnp.stack([jax.random.randint(jax.random.fold_in(_tk, 200 + f), (512,), 0, v, jnp.int32) for f, v in enumerate([12500, 12500, 1250, 1000, 1000, 125000, 1250, 1000, 1000, 12500, 12500, 1000, 12500, 12500, 12500, 12500, 1250, 12500, 1250, 1000, 1000, 1000, 1000, 1000, 1000, 1000])], axis=1)
        tbl_0 = 0.05 * jax.random.normal(jax.random.fold_in(_tk, 500 + 0), (12500, 128), jnp.float32)
        tbl_1 = 0.05 * jax.random.normal(jax.random.fold_in(_tk, 500 + 1), (12500, 128), jnp.float32)
        tbl_2 = 0.05 * jax.random.normal(jax.random.fold_in(_tk, 500 + 2), (1250, 128), jnp.float32)
        tbl_3 = 0.05 * jax.random.normal(jax.random.fold_in(_tk, 500 + 3), (1000, 128), jnp.float32)
        tbl_4 = 0.05 * jax.random.normal(jax.random.fold_in(_tk, 500 + 4), (1000, 128), jnp.float32)
        tbl_5 = 0.05 * jax.random.normal(jax.random.fold_in(_tk, 500 + 5), (125000, 128), jnp.float32)
        tbl_6 = 0.05 * jax.random.normal(jax.random.fold_in(_tk, 500 + 6), (1250, 128), jnp.float32)
        tbl_7 = 0.05 * jax.random.normal(jax.random.fold_in(_tk, 500 + 7), (1000, 128), jnp.float32)
        tbl_8 = 0.05 * jax.random.normal(jax.random.fold_in(_tk, 500 + 8), (1000, 128), jnp.float32)
        tbl_9 = 0.05 * jax.random.normal(jax.random.fold_in(_tk, 500 + 9), (12500, 128), jnp.float32)
        tbl_10 = 0.05 * jax.random.normal(jax.random.fold_in(_tk, 500 + 10), (12500, 128), jnp.float32)
        tbl_11 = 0.05 * jax.random.normal(jax.random.fold_in(_tk, 500 + 11), (1000, 128), jnp.float32)
        tbl_12 = 0.05 * jax.random.normal(jax.random.fold_in(_tk, 500 + 12), (12500, 128), jnp.float32)
        tbl_13 = 0.05 * jax.random.normal(jax.random.fold_in(_tk, 500 + 13), (12500, 128), jnp.float32)
        tbl_14 = 0.05 * jax.random.normal(jax.random.fold_in(_tk, 500 + 14), (12500, 128), jnp.float32)
        tbl_15 = 0.05 * jax.random.normal(jax.random.fold_in(_tk, 500 + 15), (12500, 128), jnp.float32)
        tbl_16 = 0.05 * jax.random.normal(jax.random.fold_in(_tk, 500 + 16), (1250, 128), jnp.float32)
        tbl_17 = 0.05 * jax.random.normal(jax.random.fold_in(_tk, 500 + 17), (12500, 128), jnp.float32)
        tbl_18 = 0.05 * jax.random.normal(jax.random.fold_in(_tk, 500 + 18), (1250, 128), jnp.float32)
        tbl_19 = 0.05 * jax.random.normal(jax.random.fold_in(_tk, 500 + 19), (1000, 128), jnp.float32)
        tbl_20 = 0.05 * jax.random.normal(jax.random.fold_in(_tk, 500 + 20), (1000, 128), jnp.float32)
        tbl_21 = 0.05 * jax.random.normal(jax.random.fold_in(_tk, 500 + 21), (1000, 128), jnp.float32)
        tbl_22 = 0.05 * jax.random.normal(jax.random.fold_in(_tk, 500 + 22), (1000, 128), jnp.float32)
        tbl_23 = 0.05 * jax.random.normal(jax.random.fold_in(_tk, 500 + 23), (1000, 128), jnp.float32)
        tbl_24 = 0.05 * jax.random.normal(jax.random.fold_in(_tk, 500 + 24), (1000, 128), jnp.float32)
        tbl_25 = 0.05 * jax.random.normal(jax.random.fold_in(_tk, 500 + 25), (1000, 128), jnp.float32)
        _rk = jax.random.fold_in(_tk, 7)
        r_dense_features = -0.000520686 + 1.00062 * jax.random.normal(jax.random.fold_in(_rk, 101), (512, 128), jnp.float32)
        W_top1 = 0.0405887 * jax.random.normal(jax.random.fold_in(_tk, 801), (607, 512), jnp.float32)
        W_top2 = 0.0441942 * jax.random.normal(jax.random.fold_in(_tk, 802), (512, 256), jnp.float32)
        W_top3 = 0.0625 * jax.random.normal(jax.random.fold_in(_tk, 803), (256, 1), jnp.float32)
        b_top1 = jnp.zeros((512,), jnp.float32)
        b_top2 = jnp.zeros((256,), jnp.float32)
        return (r_dense_features, ids, tbl_0, tbl_1, tbl_2, tbl_3, tbl_4, tbl_5, tbl_6, tbl_7, tbl_8, tbl_9, tbl_10, tbl_11, tbl_12, tbl_13, tbl_14, tbl_15, tbl_16, tbl_17, tbl_18, tbl_19, tbl_20, tbl_21, tbl_22, tbl_23, tbl_24, tbl_25, W_top1, b_top1, W_top2, b_top2, W_top3)
    r_dense_features, ids, tbl_0, tbl_1, tbl_2, tbl_3, tbl_4, tbl_5, tbl_6, tbl_7, tbl_8, tbl_9, tbl_10, tbl_11, tbl_12, tbl_13, tbl_14, tbl_15, tbl_16, tbl_17, tbl_18, tbl_19, tbl_20, tbl_21, tbl_22, tbl_23, tbl_24, tbl_25, W_top1, b_top1, W_top2, b_top2, W_top3 = _rec_inputs()

    def _L0_rec_setup():
        import jax, jax.numpy as jnp
        import numpy as np
        B, F, D = (2048, 26, 128)
        key = jax.random.key(seed)
        k1, k2 = jax.random.split(key)
        dense_features = jax.random.normal(k1, (B, D), dtype=jnp.float32)
        sparse_values = jax.random.normal(k2, (B, F, D), dtype=jnp.float32)
        return {'dense_features': dense_features, 'sparse_values': sparse_values}
    _L0_rec_all = _L0_rec_setup()
    _L0_rec_in = {k: v for k, v in _L0_rec_all.items() if k in ()}
    del _L0_rec_all
    return {'r_dense_features': r_dense_features, 'ids': ids, 'tbl_0': tbl_0, 'tbl_1': tbl_1, 'tbl_2': tbl_2, 'tbl_3': tbl_3, 'tbl_4': tbl_4, 'tbl_5': tbl_5, 'tbl_6': tbl_6, 'tbl_7': tbl_7, 'tbl_8': tbl_8, 'tbl_9': tbl_9, 'tbl_10': tbl_10, 'tbl_11': tbl_11, 'tbl_12': tbl_12, 'tbl_13': tbl_13, 'tbl_14': tbl_14, 'tbl_15': tbl_15, 'tbl_16': tbl_16, 'tbl_17': tbl_17, 'tbl_18': tbl_18, 'tbl_19': tbl_19, 'tbl_20': tbl_20, 'tbl_21': tbl_21, 'tbl_22': tbl_22, 'tbl_23': tbl_23, 'tbl_24': tbl_24, 'tbl_25': tbl_25, 'W_top1': W_top1, 'b_top1': b_top1, 'W_top2': W_top2, 'b_top2': b_top2, 'W_top3': W_top3}

def reference(r_dense_features, ids, tbl_0, tbl_1, tbl_2, tbl_3, tbl_4, tbl_5, tbl_6, tbl_7, tbl_8, tbl_9, tbl_10, tbl_11, tbl_12, tbl_13, tbl_14, tbl_15, tbl_16, tbl_17, tbl_18, tbl_19, tbl_20, tbl_21, tbl_22, tbl_23, tbl_24, tbl_25, W_top1, b_top1, W_top2, b_top2, W_top3):
    import jax
    import jax.numpy as jnp

    def _L0_rec_ref(dense_features, sparse_values):
        import jax, jax.numpy as jnp
        import numpy as np
        B, F, D = (2048, 26, 128)
        sd = jnp.einsum('bfd,bd->bf', sparse_values, dense_features)
        ss = jnp.einsum('bfd,bgd->bfg', sparse_values, sparse_values)
        iu, ju = jnp.triu_indices(F, k=1)
        pairs = ss[:, iu, ju]
        return jnp.concatenate([dense_features, sd, pairs], axis=1)
    e = jnp.stack([tbl_0[ids[:, 0]], tbl_1[ids[:, 1]], tbl_2[ids[:, 2]], tbl_3[ids[:, 3]], tbl_4[ids[:, 4]], tbl_5[ids[:, 5]], tbl_6[ids[:, 6]], tbl_7[ids[:, 7]], tbl_8[ids[:, 8]], tbl_9[ids[:, 9]], tbl_10[ids[:, 10]], tbl_11[ids[:, 11]], tbl_12[ids[:, 12]], tbl_13[ids[:, 13]], tbl_14[ids[:, 14]], tbl_15[ids[:, 15]], tbl_16[ids[:, 16]], tbl_17[ids[:, 17]], tbl_18[ids[:, 18]], tbl_19[ids[:, 19]], tbl_20[ids[:, 20]], tbl_21[ids[:, 21]], tbl_22[ids[:, 22]], tbl_23[ids[:, 23]], tbl_24[ids[:, 24]], tbl_25[ids[:, 25]]], axis=1)
    z = _L0_rec_ref(r_dense_features, e)
    z = z.reshape(z.shape[0], -1)
    h = jnp.concatenate([z, r_dense_features], axis=1)
    h = jnp.maximum(h @ W_top1 + b_top1, 0.0)
    h = jnp.maximum(h @ W_top2 + b_top2, 0.0)
    y = h @ W_top3
    return y

_drawn_inputs = setup_inputs


def setup_inputs(seed=0):
    import zlib

    import numpy as np

    out = dict(_drawn_inputs(seed))
    spreads = {'b_top1': (0.0, 0.1), 'b_top2': (0.0, 0.1)}
    factors = {}
    for name, (base, spread) in spreads.items():
        noise = np.random.default_rng([zlib.crc32(name.encode()), seed]).standard_normal(out[name].shape)
        drawn = base * np.exp(spread * noise) if base else spread * noise
        out[name] = jnp.asarray(drawn.astype(out[name].dtype))
    for name, factor in factors.items():
        out[name] = (out[name] * factor).astype(out[name].dtype)
    return out
```

```python
import concourse.bass as bass
from concourse import mybir
from contextlib import ExitStack

P = 128
B = 512
D = 128
F = 26
H1, H2 = 512, 256
CHUNKS = B // P
LOOKUP = [3, 4, 7, 8, 11, 19, 20, 21]
LROWS = 1000
KL = 8
RP = LROWS // KL
GATHER = [f for f in range(F) if f not in LOOKUP]
SLOT_FIELDS = GATHER + LOOKUP
NG, NL = len(GATHER), len(LOOKUP)
DENSE = F
SLOTS = 32
GS = 3
GROUPS = NG // GS
NJ = F
QS = 32
MM = 8
PARTS = QS // MM
FOLDW = 40
FOLD = 12
ZROWS = 14
NPAIR = F * (F - 1) // 2
NZ = F + NPAIR
KZ = NZ // 3
HOT = 10


def interaction_rows():
    pair_row, n = {}, D + F
    for i in range(F):
        for j in range(i + 1, F):
            pair_row[i, j] = n
            n += 1
    rows = []
    for r in range(ZROWS):
        for c in range(F):
            j = F - r
            if r == 0:
                rows.append(D + SLOT_FIELDS[c])
            elif c < j:
                a, b = SLOT_FIELDS[c], SLOT_FIELDS[j]
                rows.append(pair_row[min(a, b), max(a, b)])
            elif r <= FOLD:
                a, b = SLOT_FIELDS[c - j], SLOT_FIELDS[r]
                rows.append(pair_row[min(a, b), max(a, b)])
    return rows


def schedule():
    turns = [("turn", c, g) for c in range(CHUNKS) for g in range(GROUPS)]
    order = [("dense",)]
    done = 0
    for q in range(NL):
        order.append(("lookup", q))
        ready = max(0, int((q * 3.45 - 0.5) / (1.04 * GS)))
        while done < ready:
            order.append(turns[done])
            done += 1
    def grams(c):
        return [("gram", c, h) for h in range(PARTS)] + [("flip", c)]
    def top(c):
        return [("pairs", c), ("layer1", c), ("layer2", c), ("layer3", c)]
    while done < 2 * GROUPS:
        order.append(turns[done])
        done += 1
    order += grams(0)
    g1 = grams(1)
    order += g1[:1] + [("pairs", 0)] + g1[1:2] + [("layer1", 0)] + g1[2:3] + [("layer2", 0)] + g1[3:5] + [("layer3", 0)]
    order += turns[2 * GROUPS:3 * GROUPS]
    g2 = grams(2)
    order += g2[:1] + [("pairs", 1)] + g2[1:2] + [("layer1", 1)] + g2[2:3] + [("layer2", 1)] + g2[3:5] + [("layer3", 1)]
    order += turns[3 * GROUPS:4 * GROUPS - 2]
    order += top(2)
    order += turns[4 * GROUPS - 2:]
    order += grams(3) + top(3)
    return order


ORDER = schedule()
RING = {}
for _s in ORDER:
    if _s[0] in ("dense", "turn", "pairs", "layer2", "layer3"):
        RING[_s] = len(RING)


def build(nc, ids_gather, ids_lookup, row_ids, identity, dense, tables, w_pairs, w_dense, w2, w3, b1, b2, out):
    f32, f32r, i32 = mybir.dt.float32, mybir.dt.float32r, mybir.dt.int32
    ALU = mybir.AluOpType
    ACT = mybir.ActivationFunctionType

    with ExitStack() as ctx:
        def sb(name, shape, dt=f32):
            return ctx.enter_context(nc.sbuf_tensor(name, shape, dt))

        def pb(name, shape):
            return ctx.enter_context(nc.psum_tensor(name, shape, f32))

        def sem(name):
            return ctx.enter_context(nc.semaphore(name))

        featT = sb("featT", [P, B, SLOTS])
        rows = sb("rows", [P, CHUNKS, NG, D])
        idx = sb("idx", [P, CHUNKS, NG], i32)
        want = sb("want", [P, NL, B], i32)
        rowid = sb("rowid", [P, KL])
        ident = sb("ident", [P, P])
        dense_rows = sb("dense_rows", [P, CHUNKS, D])
        denseT = sb("denseT", [P, CHUNKS, 4, QS])
        table = sb("table", [P, 2, KL, D])
        high = sb("high", [P, 2, KL, D], f32r)
        low = sb("low", [P, 2, KL, D], f32r)
        hot = sb("hot", [P, HOT, B], f32r)
        wp = sb("wp", [P, 3, H1])
        wd = sb("wd", [P, 2, H1])
        wds = sb("wds", [P, H1])
        w2s = sb("w2s", [P, H1 // P, H2])
        w3s = sb("w3s", [P, H2 // P])
        b1s = sb("b1s", [P, H1 // P])
        b2s = sb("b2s", [P, H2 // P])
        gram_rows = sb("gram_rows", [P, 2, QS, NJ])
        flipped = sb("flipped", [P, NJ, FOLDW])
        inter = sb("inter", [P, 2, ZROWS, F])
        interT = sb("interT", [P, 2, 3, P])
        hid1 = sb("hid1", [P, 2, H1 // P, P])
        hid2 = sb("hid2", [P, 2, H2 // P, P])
        y = sb("y", [1, B])

        ring = [pb(f"ring{i}", [P, 512]) for i in range(2)]
        gram = [pb(f"gram{i}", [P, MM, P]) for i in range(2)]
        wide = [pb(f"wide{i}", [P, 512]) for i in range(2)]

        idx_loaded = sem("idx_loaded")
        want_loaded = [sem(f"want_loaded{i}") for i in range(2)]
        rowid_loaded = sem("rowid_loaded")
        ident_loaded = sem("ident_loaded")
        dense_loaded = sem("dense_loaded")
        table_loaded = [sem(f"table_loaded{q}") for q in range(NL)]
        wp_loaded = sem("wp_loaded")
        wd_loaded = sem("wd_loaded")
        w2_loaded = sem("w2_loaded")
        small_loaded = sem("small_loaded")
        gathered = [[sem(f"gathered{c}_{g}") for g in range(GROUPS)] for c in range(CHUNKS)]
        pads_zero = sem("pads_zero")
        wds_ready = sem("wds_ready")
        hot_ready = sem("hot_ready")
        high_ready = sem("high_ready")
        low_ready = sem("low_ready")
        hot_used = sem("hot_used")
        looked_up = sem("looked_up")
        ring_full = sem("ring_full")
        ring_dve = sem("ring_dve")
        ring_act = sem("ring_act")
        gram_full = sem("gram_full")
        gram_dve = sem("gram_dve")
        gram_act = sem("gram_act")
        flip_done = sem("flip_done")
        fold_done = sem("fold_done")
        inter_ready = sem("inter_ready")
        wide0_full = sem("wide0_full")
        wide1_full = sem("wide1_full")
        hid1_act = sem("hid1_act")
        hid1_dve = sem("hid1_dve")
        stored = sem("stored")
        block = ctx.enter_context(nc.Block())

        last_chunk_entry = {c: RING[("turn", c, GROUPS - 1)] for c in range(CHUNKS)}

        def wait_ring_out(eng, n):
            eng.wait_ge(ring_act if n % 2 else ring_dve, n // 2 + 1)

        @block.sync
        def _(sp):
            sp.dma_start(idx[:], ids_gather).then_inc(idx_loaded, 16)
            sp.dma_start(rowid[:], row_ids).then_inc(rowid_loaded, 16)
            sp.dma_start(want[:, 0:2, :], ids_lookup[:, 0:2, :]).then_inc(want_loaded[0], 16)

            def load_table(q):
                if q >= 2:
                    sp.wait_ge(high_ready, q - 1)
                    sp.wait_ge(low_ready, q - 1)
                src = tables[SLOT_FIELDS[NG + q]].rearrange("(p k) d -> p k d", k=KL)
                sp.dma_start(table[0:112, q % 2], src[0:112]).then_inc(table_loaded[q], 16)
                sp.dma_start(table[112:RP, q % 2], src[112:RP]).then_inc(table_loaded[q], 16)

            load_table(0)
            sp.dma_start(ident[:], identity).then_inc(ident_loaded, 16)
            sp.dma_start(dense_rows[:], dense.rearrange("(c p) d -> p c d", p=P)).then_inc(dense_loaded, 16)
            load_table(1)
            sp.dma_start(want[:, 2:NL, :], ids_lookup[:, 2:NL, :]).then_inc(want_loaded[1], 16)
            for q in range(2, NL):
                load_table(q)
            sp.dma_start(wp[0:KZ], w_pairs).then_inc(wp_loaded, 16)
            sp.dma_start(wd[:], w_dense).then_inc(wd_loaded, 16)
            sp.dma_start(w2s[:], w2.rearrange("(k p) n -> p k n", p=P)).then_inc(w2_loaded, 16)
            sp.dma_start(w3s[:], w3).then_inc(small_loaded, 16)
            sp.dma_start(b1s[:], b1).then_inc(small_loaded, 16)
            sp.dma_start(b2s[:], b2).then_inc(small_loaded, 16)
            wait_ring_out(sp, RING[("layer3", CHUNKS - 1)])
            wait_ring_out(sp, RING[("layer3", CHUNKS - 2)])
            sp.dma_start(out, y[:]).then_inc(stored, 16)
            sp.wait_ge(stored, 16)

        @block.gpsimd
        def _(pool):
            pool.wait_ge(idx_loaded, 16)
            for c in range(CHUNKS):
                for f in range(NG):
                    pool.indirect_dma_start(
                        rows[:, c, f, :], None, tables[GATHER[f]],
                        bass.IndirectOffsetOnAxis(ap=idx[:, c, f:f + 1], axis=0),
                    ).then_inc(gathered[c][f // GS], 16)

        @block.tensor
        def _(pe):
            def ring_bank(s):
                n = RING[s]
                if n >= 2:
                    wait_ring_out(pe, n - 2)
                return ring[n % 2]

            def do_dense():
                pe.wait_ge(ident_loaded, 16)
                pe.wait_ge(dense_loaded, 16)
                bank = ring_bank(("dense",))
                for c in range(CHUNKS):
                    last = nc.tensor.transpose(bank[:, c * P:(c + 1) * P], dense_rows[:, c, :], ident[:])
                last.then_inc(ring_full, 1)

            def do_turn(c, g):
                bank = ring_bank(("turn", c, g))
                pe.wait_ge(gathered[c][g], 16 * GS)
                for e in range(GS):
                    last = nc.tensor.transpose(bank[:, e * P:(e + 1) * P], rows[:, c, g * GS + e, :], ident[:])
                last.then_inc(ring_full, 1)

            def do_lookup(q):
                if q >= 2:
                    pe.wait_ge(looked_up, q - 1)
                pe.wait_ge(high_ready, q + 1)
                pe.wait_ge(low_ready, q + 1)
                for k in range(KL):
                    pe.wait_ge(hot_ready, q * KL + k + 1)
                    mov = hot[0:RP, (q * KL + k) % HOT, :]
                    nc.tensor.matmul(wide[q % 2][:], high[0:RP, q % 2, k, :], mov, start=(k == 0), stop=False)
                    nc.tensor.matmul(wide[q % 2][:], low[0:RP, q % 2, k, :], mov, start=False,
                                     stop=(k == KL - 1)).then_inc(hot_used, 1)

            def do_gram(c, h):
                n = c * PARTS + h
                if h == 0:
                    wait_ring_out(pe, last_chunk_entry[c])
                    wait_ring_out(pe, last_chunk_entry[c] - 1)
                    if c == 0:
                        pe.wait_ge(looked_up, NL)
                        pe.wait_ge(pads_zero, 1)
                if n >= 2:
                    pe.wait_ge(gram_dve, n - 1)
                    pe.wait_ge(gram_act, n - 1)
                for m in range(MM):
                    s = c * P + 4 * (h * MM + m)
                    last = nc.tensor.matmul(gram[n % 2][:, m, 0:4 * NJ],
                                            featT[:, s:s + 4, :].rearrange("p s j -> p (s j)"),
                                            featT[:, s:s + 4, 1:1 + NJ], start=True, stop=True)
                last.then_inc(gram_full, 1)

            def do_pairs(c):
                bank = ring_bank(("pairs", c))
                pe.wait_ge(inter_ready, c + 1)
                z = inter[:, c % 2].rearrange("p r j -> p (r j)")
                for t in range(3):
                    last = nc.tensor.transpose(bank[0:KZ, t * P:(t + 1) * P], z[:, t * KZ:(t + 1) * KZ], ident[:])
                last.then_inc(ring_full, 1)

            def do_layer1(c):
                if c == 0:
                    pe.wait_ge(wp_loaded, 16)
                    pe.wait_ge(wds_ready, 1)
                    pe.wait_ge(looked_up, NL)
                wait_ring_out(pe, RING[("pairs", c)])
                for m in range(H1 // P):
                    if c >= 1 and m == 0:
                        pe.wait_ge(hid1_act, c)
                    if c >= 1 and m == 2:
                        pe.wait_ge(hid1_dve, c)
                    o = wide[m // 2][:, (m % 2) * P:(m % 2 + 1) * P]
                    cols = slice(m * P, (m + 1) * P)
                    nc.tensor.matmul(o, wds[:, cols], denseT[:, c].rearrange("p s g -> p (s g)"), start=True, stop=False)
                    for t in range(3):
                        last = nc.tensor.matmul(o, wp[0:KZ, t, cols], interT[0:KZ, c % 2, t, :],
                                                start=False, stop=(t == 2))
                    if m % 2:
                        last.then_inc([wide0_full, wide1_full][m // 2], 1)

            def do_layer2(c):
                bank = ring_bank(("layer2", c))
                if c == 0:
                    pe.wait_ge(w2_loaded, 16)
                pe.wait_ge(hid1_act, c + 1)
                pe.wait_ge(hid1_dve, c + 1)
                for m in range(H2 // P):
                    for k in range(H1 // P):
                        last = nc.tensor.matmul(bank[:, m * P:(m + 1) * P], w2s[:, k, m * P:(m + 1) * P],
                                                hid1[:, c % 2, k, :], start=(k == 0), stop=(k == H1 // P - 1))
                last.then_inc(ring_full, 1)

            def do_layer3(c):
                bank = ring_bank(("layer3", c))
                if c == 0:
                    pe.wait_ge(small_loaded, 48)
                wait_ring_out(pe, RING[("layer2", c)])
                for k in range(H2 // P):
                    last = nc.tensor.matmul(bank[0:1, 0:P], w3s[:, k:k + 1], hid2[:, c % 2, k, :],
                                            start=(k == 0), stop=(k == H2 // P - 1))
                last.then_inc(ring_full, 1)

            steps = {"dense": do_dense, "turn": do_turn, "lookup": do_lookup, "gram": do_gram,
                     "pairs": do_pairs, "layer1": do_layer1, "layer2": do_layer2, "layer3": do_layer3}
            for kind, *at in ORDER:
                if kind in steps:
                    steps[kind](*at)

        def feat_slots(c, g):
            return featT[:, c * P:(c + 1) * P, g * GS:(g + 1) * GS].rearrange("p b j -> p j b")

        @block.scalar
        def _(act):
            def split_high(q):
                act.wait_ge(table_loaded[q], 32)
                if q >= 2:
                    act.wait_ge(hot_used, KL * (q - 1))
                nc.scalar.activation(high[0:RP, q % 2], table[0:RP, q % 2], ACT.Copy).then_inc(high_ready, 1)

            split_high(0)
            for s in ORDER:
                kind, at = s[0], s[1:]
                if kind == "lookup":
                    q, = at
                    if q + 1 < NL:
                        split_high(q + 1)
                    act.wait_ge(hot_used, KL * (q + 1))
                    nc.scalar.activation(featT[:, :, NG + q], wide[q % 2][:], ACT.Copy).then_inc(looked_up, 1)
                elif kind == "gram":
                    c, h = at
                    n = c * PARTS + h
                    act.wait_ge(gram_full, n + 1)
                    if c >= 2 and h == 0:
                        act.wait_ge(flip_done, c - 1)
                    for s4 in range(2):
                        part = slice(s4 * QS, (s4 + 1) * QS)
                        last = nc.scalar.activation(gram_rows[part, c % 2, h * MM:(h + 1) * MM, :],
                                                    gram[n % 2][part, :, s4 * NJ:(s4 + 1) * NJ], ACT.Copy)
                    last.then_inc(gram_act, 1)
                elif kind == "layer1":
                    c, = at
                    if c == 0:
                        act.wait_ge(small_loaded, 48)
                    act.wait_ge(wide0_full, c + 1)
                    if c >= 2:
                        act.wait_ge(ring_full, RING[("layer2", c - 2)] + 1)
                    for m in range(2):
                        last = nc.scalar.activation(hid1[:, c % 2, m, :], wide[0][:, m * P:(m + 1) * P],
                                                    ACT.Relu, bias=b1s[:, m:m + 1])
                    last.then_inc(hid1_act, 1)
                elif s in RING and RING[s] % 2:
                    n = RING[s]
                    bank = ring[1]
                    act.wait_ge(ring_full, n + 1)
                    if kind == "turn":
                        nc.scalar.activation(feat_slots(*at), bank[:, 0:GS * P].rearrange("p (j b) -> p j b", b=P),
                                             ACT.Copy).then_inc(ring_act, 1)
                    elif kind == "pairs":
                        c, = at
                        if c >= 2:
                            act.wait_ge(wide1_full, c - 1)
                        nc.scalar.activation(interT[0:KZ, c % 2], bank[0:KZ, 0:3 * P].rearrange("p (t b) -> p t b", b=P),
                                             ACT.Copy).then_inc(ring_act, 1)
                    elif kind == "layer2":
                        c, = at
                        if c >= 2:
                            act.wait_ge(ring_full, RING[("layer3", c - 2)] + 1)
                        for m in range(H2 // P):
                            last = nc.scalar.activation(hid2[:, c % 2, m, :], bank[:, m * P:(m + 1) * P],
                                                        ACT.Relu, bias=b2s[:, m:m + 1])
                        last.then_inc(ring_act, 1)
                    elif kind == "layer3":
                        c, = at
                        nc.scalar.activation(y[0:1, c * P:(c + 1) * P].rearrange("o (g s) -> o s g", s=4),
                                             bank[0:1, 0:P].rearrange("o (s g) -> o s g", s=4),
                                             ACT.Copy).then_inc(ring_act, 1)

        @block.vector
        def _(dve):
            def make_hot(q):
                if q == 0:
                    dve.wait_ge(rowid_loaded, 16)
                    dve.wait_ge(want_loaded[0], 16)
                if q == 2:
                    dve.wait_ge(want_loaded[1], 16)
                for k in range(KL):
                    n = q * KL + k
                    if n >= HOT:
                        dve.wait_ge(hot_used, n - HOT + 1)
                    nc.vector.tensor_scalar(hot[0:RP, n % HOT, :], want[0:RP, q, :], rowid[0:RP, k:k + 1], None,
                                            ALU.is_equal).then_inc(hot_ready, 1)
                    if k == 1:
                        split_low(q)

            def split_low(q):
                dve.wait_ge(high_ready, q + 1)
                if q >= 2:
                    dve.wait_ge(hot_used, KL * (q - 1))
                nc.vector.tensor_tensor(low[0:RP, q % 2], table[0:RP, q % 2], high[0:RP, q % 2].bitcast(f32),
                                        ALU.subtract).then_inc(low_ready, 1)

            make_hot(0)
            for s in ORDER:
                kind, at = s[0], s[1:]
                if kind == "dense":
                    assert RING[s] == 0
                    dve.wait_ge(ring_full, 1)
                    nc.vector.tensor_copy(featT[:, :, DENSE], ring[0][:])
                    nc.vector.tensor_copy(denseT[:], ring[0][:].rearrange("p (c g s) -> p c s g", c=CHUNKS, s=4)
                                          ).then_inc(ring_dve, 1)
                elif kind == "lookup":
                    q, = at
                    if q + 1 < NL:
                        make_hot(q + 1)
                    if q == NL - 1:
                        nc.vector.memset(featT[:, :, DENSE + 1:SLOTS], 0.0).then_inc(pads_zero, 1)
                        dve.wait_ge(wd_loaded, 16)
                        nc.vector.tensor_tensor(wds[:], wd[:, 0, :], wd[:, 1, :], ALU.add).then_inc(wds_ready, 1)
                elif kind == "gram":
                    c, h = at
                    n = c * PARTS + h
                    dve.wait_ge(gram_full, n + 1)
                    if c >= 2 and h == 0:
                        dve.wait_ge(flip_done, c - 1)
                    for s4 in range(2, 4):
                        part = slice(s4 * QS, (s4 + 1) * QS)
                        last = nc.vector.tensor_copy(gram_rows[part, c % 2, h * MM:(h + 1) * MM, :],
                                                     gram[n % 2][part, :, s4 * NJ:(s4 + 1) * NJ])
                    last.then_inc(gram_dve, 1)
                elif kind == "flip":
                    c, = at
                    dve.wait_ge(gram_act, PARTS * (c + 1))
                    dve.wait_ge(gram_dve, PARTS * (c + 1))
                    if c >= 1:
                        dve.wait_ge(inter_ready, c)
                    nc.vector.transpose(flipped[:, :, 0:SLOTS], gram_rows[:, c % 2].rearrange("p g j -> p j g")
                                        ).then_inc(flip_done, 1)
                    dve.wait_ge(flip_done, c + 1)
                    flat = flipped[:].rearrange("p j i -> p (j i)")
                    first = (F - 2) * FOLDW + F - 1
                    fold_out = flat[:, first:first + 1]
                    fold_out = bass.AP(tensor=fold_out.tensor, offset=fold_out.offset,
                                       ap=[list(fold_out.ap[0]), [-(FOLDW + 1), FOLD], [1, FOLD]])
                    nc.vector.tensor_copy(fold_out, flipped[:, 0:FOLD, 0:FOLD]).then_inc(fold_done, 1)
                    dve.wait_ge(fold_done, c + 1)
                    if c >= 2:
                        dve.wait_ge(ring_full, RING[("pairs", c - 2)] + 1)
                    lo = NJ - ZROWS
                    nc.vector.tensor_copy(inter[:, c % 2], flipped[:, NJ - 1:lo - 1:-1, 0:F]).then_inc(inter_ready, 1)
                elif kind == "layer1":
                    c, = at
                    if c == 0:
                        dve.wait_ge(small_loaded, 48)
                    dve.wait_ge(wide1_full, c + 1)
                    if c >= 2:
                        dve.wait_ge(ring_full, RING[("layer2", c - 2)] + 1)
                    for m in range(2, 4):
                        last = nc.vector.tensor_scalar(hid1[:, c % 2, m, :], wide[1][:, (m - 2) * P:(m - 1) * P],
                                                       b1s[:, m:m + 1], 0.0, ALU.add, ALU.max)
                    last.then_inc(hid1_dve, 1)
                elif s in RING and RING[s] % 2 == 0:
                    n = RING[s]
                    bank = ring[0]
                    dve.wait_ge(ring_full, n + 1)
                    if kind == "turn":
                        nc.vector.tensor_copy(feat_slots(*at), bank[:, 0:GS * P].rearrange("p (j b) -> p j b", b=P)
                                              ).then_inc(ring_dve, 1)
                    elif kind == "pairs":
                        c, = at
                        if c >= 2:
                            dve.wait_ge(wide1_full, c - 1)
                        nc.vector.tensor_copy(interT[0:KZ, c % 2], bank[0:KZ, 0:3 * P].rearrange("p (t b) -> p t b", b=P)
                                              ).then_inc(ring_dve, 1)
                    elif kind == "layer2":
                        c, = at
                        if c >= 2:
                            dve.wait_ge(ring_full, RING[("layer3", c - 2)] + 1)
                        for m in range(H2 // P):
                            last = nc.vector.tensor_scalar(hid2[:, c % 2, m, :], bank[:, m * P:(m + 1) * P],
                                                           b2s[:, m:m + 1], 0.0, ALU.add, ALU.max)
                        last.then_inc(ring_dve, 1)
                    elif kind == "layer3":
                        c, = at
                        nc.vector.tensor_copy(y[0:1, c * P:(c + 1) * P].rearrange("o (g s) -> o s g", s=4),
                                              bank[0:1, 0:P].rearrange("o (s g) -> o s g", s=4)).then_inc(ring_dve, 1)


def kernel(**inputs):
    import numpy as np
    import concourse.bacc as bacc
    from concourse.bass_utils import run_bass_kernel_spmd

    ids = np.asarray(inputs["ids"])
    w1 = np.asarray(inputs["W_top1"])
    arrays = {
        "ids_gather": ids[:, GATHER].reshape(CHUNKS, P, NG).transpose(1, 0, 2),
        "ids_lookup": ids[:, LOOKUP].T[None],
        "row_ids": np.pad(np.arange(LROWS, dtype=np.float32).reshape(RP, KL), ((0, P - RP), (0, 0)), constant_values=-1),
        "identity": np.eye(P, dtype=np.float32),
        "dense": inputs["r_dense_features"],
        "w_pairs": w1[interaction_rows()].reshape(3, KZ, H1).transpose(1, 0, 2),
        "w_dense": np.stack([w1[0:D], w1[D + NZ:]], axis=1),
        "w2": inputs["W_top2"],
        "w3": np.asarray(inputs["W_top3"]).reshape(H2 // P, P).T,
        "b1": np.asarray(inputs["b_top1"]).reshape(H1 // P, P).T,
        "b2": np.asarray(inputs["b_top2"]).reshape(H2 // P, P).T,
    }
    for f in range(F):
        arrays[f"tbl_{f}"] = inputs[f"tbl_{f}"]
    arrays = {name: np.ascontiguousarray(a) for name, a in arrays.items()}

    nc = bacc.Bacc("TRN2", target_bir_lowering=False, num_devices=1)
    aps = {name: nc.dram_tensor(name, a.shape, mybir.dt.from_np(a.dtype), kind="ExternalInput").ap()
           for name, a in arrays.items()}
    out = nc.dram_tensor("out", (1, B), mybir.dt.float32, kind="ExternalOutput").ap()
    build(nc, aps["ids_gather"], aps["ids_lookup"].to_broadcast([P, NL, B]), aps["row_ids"], aps["identity"], aps["dense"],
          [aps[f"tbl_{f}"] for f in range(F)], aps["w_pairs"], aps["w_dense"], aps["w2"], aps["w3"],
          aps["b1"], aps["b2"], out)
    r = run_bass_kernel_spmd(nc, [arrays], core_ids=[0])
    return r.results[0]["out"].reshape(B, 1)
```

```python
import concourse.bass as bass
from concourse import mybir
from contextlib import ExitStack

P = 128
B = 512
D = 128
F = 26
H1, H2 = 512, 256
CHUNKS = B // P
LOOKUP = [3, 4, 7, 8, 11, 19, 20, 21]
LROWS = 1000
KL = 8
RP = LROWS // KL
GATHER = [f for f in range(F) if f not in LOOKUP]
SLOT_FIELDS = GATHER + LOOKUP
NG, NL = len(GATHER), len(LOOKUP)
DENSE = F
SLOTS = 32
GROUPS = -(-NG // 4)
GROUP_AT = [NG - NG * (GROUPS - g) // GROUPS for g in range(GROUPS + 1)]
GROUP_OF = [g for g in range(GROUPS) for _ in range(GROUP_AT[g], GROUP_AT[g + 1])]
NJ = F
QS = 32
MM = 8
PARTS = QS // MM
FOLDW = 40
FOLD = 12
ZROWS = 14
NPAIR = F * (F - 1) // 2
NZ = F + NPAIR
WARM = 14
KZ = NZ // 3
ROWBUFS = 3
HOT = 12
KV = 6


def interaction_rows():
    pair_row, n = {}, D + F
    for i in range(F):
        for j in range(i + 1, F):
            pair_row[i, j] = n
            n += 1
    rows = []
    for r in range(ZROWS):
        for c in range(F):
            j = F - r
            if r == 0:
                rows.append(D + SLOT_FIELDS[c])
            elif c < j:
                a, b = SLOT_FIELDS[c], SLOT_FIELDS[j]
                rows.append(pair_row[min(a, b), max(a, b)])
            elif r <= FOLD:
                a, b = SLOT_FIELDS[c - j], SLOT_FIELDS[r]
                rows.append(pair_row[min(a, b), max(a, b)])
    return rows


def schedule():
    cost = {"lookup": 3.6, "gram": 1.4, "pairs": 0.3, "dense1": 0.9, "layer1": 2.6, "layer2": 1.7, "layer3": 0.4}
    turns = [("turn", c, g) for c in range(CHUNKS) for g in range(GROUPS)]
    order, clock, done = [], 6.5, 0

    def ready(n):
        return 5.5 + 1.04 * (n // GROUPS * NG + GROUP_AT[n % GROUPS + 1])

    main = [("lookup", q) for q in range(NL)]
    for c in range(CHUNKS):
        main += [("gram", c, h) for h in range(PARTS)] + [("flip", c)]
        main += [("layer2", c - 1)] * (c > 0) + [("dense1", c), ("pairs", c)] + [("layer3", c - 1)] * (c > 0)
        main += [("layer1", c)]
    main += [("layer2", c), ("layer3", c)]
    for s in main:
        if s[0] == "gram" and s[2] == 0:
            needed = (s[1] + 1) * GROUPS
        else:
            needed = 0
        while done < len(turns) and (done < needed or ready(done) <= clock):
            clock = max(clock, ready(done)) + 0.3
            order.append(turns[done])
            done += 1
        order.append(s)
        if s == ("lookup", 0):
            order.append(("dense",))
        clock += cost.get(s[0], 0)
    return order


ORDER = schedule()
RING = {}
for _s in ORDER:
    if _s[0] in ("dense", "turn", "pairs", "layer2", "layer3"):
        RING[_s] = len(RING)


def build(nc, ids_gather, ids_lookup, row_ids, identity, dense, tables, w_pairs, w_dense, w2, w3, b1, b2, out):
    f32, f32r, i32 = mybir.dt.float32, mybir.dt.float32r, mybir.dt.int32
    ALU = mybir.AluOpType
    ACT = mybir.ActivationFunctionType

    with ExitStack() as ctx:
        def sb(name, shape, dt=f32):
            return ctx.enter_context(nc.sbuf_tensor(name, shape, dt))

        def pb(name, shape):
            return ctx.enter_context(nc.psum_tensor(name, shape, f32))

        def sem(name):
            return ctx.enter_context(nc.semaphore(name))

        featT = sb("featT", [P, B, SLOTS])
        rows = sb("rows", [P, ROWBUFS, NG, D])
        idx = sb("idx", [P, CHUNKS, NG], i32)
        want = sb("want", [P, NL, B], i32)
        rowid = sb("rowid", [P, KL])
        ident = sb("ident", [P, P])
        dense_rows = sb("dense_rows", [P, CHUNKS, D])
        denseT = sb("denseT", [P, CHUNKS, 4, QS])
        table = sb("table", [P, 2, KL, D])
        high = sb("high", [P, 2, KL, D], f32r)
        low = sb("low", [P, 2, KL, D], f32r)
        hot = sb("hot", [P, HOT, B], f32r)
        apart = sb("apart", [P, KL - KV, B])
        wp = sb("wp", [P, 3, H1])
        wd = sb("wd", [P, 2, H1])
        wds = sb("wds", [P, H1])
        w2s = sb("w2s", [P, H1 // P, H2])
        w3s = sb("w3s", [P, H2 // P])
        b1s = sb("b1s", [P, H1 // P])
        b2s = sb("b2s", [P, H2 // P])
        gram_rows = sb("gram_rows", [P, 2, QS, NJ])
        flipped = sb("flipped", [P, NJ, FOLDW])
        inter = sb("inter", [P, 2, ZROWS, F])
        interT = sb("interT", [P, 2, 3, P])
        hid1 = sb("hid1", [P, 2, H1 // P, P])
        hid2 = sb("hid2", [P, 2, H2 // P, P])
        y = sb("y", [1, B])
        idle = sb("idle", [P, B], mybir.dt.bfloat16)

        ring = [pb(f"ring{i}", [P, 512]) for i in range(2)]
        gram = [pb(f"gram{i}", [P, MM, P]) for i in range(2)]
        wide = [pb(f"wide{i}", [P, 512]) for i in range(2)]

        idx_loaded = sem("idx_loaded")
        want_loaded = [sem(f"want_loaded{q}") for q in range(NL)]
        rowid_loaded = sem("rowid_loaded")
        ident_loaded = sem("ident_loaded")
        dense_loaded = sem("dense_loaded")
        table_loaded = [sem(f"table_loaded{q}") for q in range(NL)]
        wp_loaded = sem("wp_loaded")
        wd_loaded = sem("wd_loaded")
        w2_loaded = sem("w2_loaded")
        small_loaded = sem("small_loaded")
        gathered = [[sem(f"gathered{c}_{g}") for g in range(GROUPS)] for c in range(CHUNKS)]
        idle_zero = sem("idle_zero")
        pads_zero = sem("pads_zero")
        wds_ready = sem("wds_ready")
        hot_dve = sem("hot_dve")
        hot_act = sem("hot_act")
        apart_done = sem("apart_done")
        high_ready = sem("high_ready")
        low_ready = sem("low_ready")
        hot_used = sem("hot_used")
        looked_up = sem("looked_up")
        ring_full = sem("ring_full")
        ring_dve = sem("ring_dve")
        ring_act = sem("ring_act")
        gram_full = sem("gram_full")
        gram_dve = sem("gram_dve")
        gram_act = sem("gram_act")
        flip_done = sem("flip_done")
        fold_done = sem("fold_done")
        inter_ready = sem("inter_ready")
        wide0_full = sem("wide0_full")
        wide1_full = sem("wide1_full")
        hid1_act = sem("hid1_act")
        hid1_dve = sem("hid1_dve")
        stored = sem("stored")
        block = ctx.enter_context(nc.Block())

        last_chunk_entry = {c: RING[("turn", c, GROUPS - 1)] for c in range(CHUNKS)}

        def wait_ring_out(eng, n):
            eng.wait_ge(ring_act if n % 2 else ring_dve, n // 2 + 1)

        def halves(q):
            return q + 2

        def steps_of(q):
            return [slice(0, KL // 2), slice(KL // 2, KL)] if q == 0 else [slice(0, KL)]

        @block.sync
        def _(sp):
            sp.dma_start(idx[:], ids_gather).then_inc(idx_loaded, 16)

            def load_table(q):
                if q >= 2:
                    sp.wait_ge(high_ready, halves(q - 2))
                    sp.wait_ge(low_ready, halves(q - 2))
                src = tables[SLOT_FIELDS[NG + q]].rearrange("(p k) d -> p k d", k=KL)
                sp.dma_start(table[0:112, q % 2], src[0:112]).then_inc(table_loaded[q], 16)
                sp.dma_start(table[112:RP, q % 2], src[112:RP]).then_inc(table_loaded[q], 16)
                sp.dma_start(want[:, q, :], ids_lookup[:, q, :]).then_inc(want_loaded[q], 16)

            load_table(0)
            sp.dma_start(rowid[:], row_ids).then_inc(rowid_loaded, 16)
            load_table(1)
            sp.dma_start(ident[:], identity).then_inc(ident_loaded, 16)
            sp.dma_start(dense_rows[:], dense.rearrange("(c p) d -> p c d", p=P)).then_inc(dense_loaded, 16)
            for q in range(2, NL):
                load_table(q)
            sp.dma_start(wp[0:KZ], w_pairs).then_inc(wp_loaded, 16)
            sp.dma_start(wd[:], w_dense).then_inc(wd_loaded, 16)
            sp.dma_start(w2s[:], w2.rearrange("(k p) n -> p k n", p=P)).then_inc(w2_loaded, 16)
            sp.dma_start(w3s[:], w3).then_inc(small_loaded, 16)
            sp.dma_start(b1s[:], b1).then_inc(small_loaded, 16)
            sp.dma_start(b2s[:], b2).then_inc(small_loaded, 16)
            wait_ring_out(sp, RING[("layer3", CHUNKS - 1)])
            wait_ring_out(sp, RING[("layer3", CHUNKS - 2)])
            sp.dma_start(out, y[:]).then_inc(stored, 16)
            sp.wait_ge(stored, 16)

        @block.gpsimd
        def _(pool):
            pool.wait_ge(idx_loaded, 16)
            for c in range(CHUNKS):
                for f in range(NG):
                    if c >= ROWBUFS and f in GROUP_AT:
                        pool.wait_ge(ring_full, RING[("turn", c - ROWBUFS, GROUP_OF[f])] + 1)
                    pool.indirect_dma_start(
                        rows[:, c % ROWBUFS, f, :], None, tables[GATHER[f]],
                        bass.IndirectOffsetOnAxis(ap=idx[:, c, f:f + 1], axis=0),
                    ).then_inc(gathered[c][GROUP_OF[f]], 16)

        @block.tensor
        def _(pe):
            def ring_bank(s):
                n = RING[s]
                if n >= 2:
                    wait_ring_out(pe, n - 2)
                return ring[n % 2]

            def do_dense():
                pe.wait_ge(ident_loaded, 16)
                pe.wait_ge(dense_loaded, 16)
                bank = ring_bank(("dense",))
                for c in range(CHUNKS):
                    last = nc.tensor.transpose(bank[:, c * P:(c + 1) * P], dense_rows[:, c, :], ident[:])
                last.then_inc(ring_full, 1)

            def do_turn(c, g):
                bank = ring_bank(("turn", c, g))
                pe.wait_ge(gathered[c][g], 16 * (GROUP_AT[g + 1] - GROUP_AT[g]))
                for e, f in enumerate(range(GROUP_AT[g], GROUP_AT[g + 1])):
                    last = nc.tensor.transpose(bank[:, e * P:(e + 1) * P], rows[:, c % ROWBUFS, f, :], ident[:])
                last.then_inc(ring_full, 1)

            def do_lookup(q):
                if q >= 2:
                    pe.wait_ge(looked_up, q - 1)
                for k in range(KL):
                    if k == 0 or (q == 0 and k == KL // 2):
                        ready = halves(q) - (q == 0 and k == 0)
                        pe.wait_ge(high_ready, ready)
                        pe.wait_ge(low_ready, ready)
                    if k < KV:
                        pe.wait_ge(hot_dve, q * KV + k + 1)
                    else:
                        pe.wait_ge(hot_act, q * (KL - KV) + k - KV + 1)
                    mov = hot[0:RP, (q * KL + k) % HOT, :]
                    nc.tensor.matmul(wide[q % 2][:], high[0:RP, q % 2, k, :], mov, start=(k == 0), stop=False)
                    nc.tensor.matmul(wide[q % 2][:], low[0:RP, q % 2, k, :], mov, start=False,
                                     stop=(k == KL - 1)).then_inc(hot_used, 1)

            def do_gram(c, h):
                n = c * PARTS + h
                if h == 0:
                    wait_ring_out(pe, last_chunk_entry[c])
                    wait_ring_out(pe, last_chunk_entry[c] - 1)
                    if c == 0:
                        pe.wait_ge(looked_up, NL)
                        pe.wait_ge(pads_zero, 1)
                if n >= 2:
                    pe.wait_ge(gram_dve, n - 1)
                    pe.wait_ge(gram_act, n - 1)
                for m in range(MM):
                    s = c * P + 4 * (h * MM + m)
                    last = nc.tensor.matmul(gram[n % 2][:, m, 0:4 * NJ],
                                            featT[:, s:s + 4, :].rearrange("p s j -> p (s j)"),
                                            featT[:, s:s + 4, 1:1 + NJ], start=True, stop=True)
                last.then_inc(gram_full, 1)

            def do_pairs(c):
                bank = ring_bank(("pairs", c))
                pe.wait_ge(inter_ready, c + 1)
                z = inter[:, c % 2].rearrange("p r j -> p (r j)")
                for t in range(3):
                    last = nc.tensor.transpose(bank[0:KZ, t * P:(t + 1) * P], z[:, t * KZ:(t + 1) * KZ], ident[:])
                last.then_inc(ring_full, 1)

            def do_dense1(c):
                if c == 0:
                    pe.wait_ge(wds_ready, 1)
                    pe.wait_ge(looked_up, NL)
                for m in range(H1 // P):
                    if c >= 1 and m == 0:
                        pe.wait_ge(hid1_act, c)
                    if c >= 1 and m == 2:
                        pe.wait_ge(hid1_dve, c)
                    nc.tensor.matmul(wide[m // 2][:, (m % 2) * P:(m % 2 + 1) * P], wds[:, m * P:(m + 1) * P],
                                     denseT[:, c].rearrange("p s g -> p (s g)"),
                                     start=(m % 2 == 0), stop=False, skip_group_check=True)

            def do_layer1(c):
                if c == 0:
                    pe.wait_ge(wp_loaded, 16)
                wait_ring_out(pe, RING[("pairs", c)])
                for m in range(H1 // P):
                    for t in range(3):
                        last = nc.tensor.matmul(wide[m // 2][:, (m % 2) * P:(m % 2 + 1) * P],
                                                wp[0:KZ, t, m * P:(m + 1) * P], interT[0:KZ, c % 2, t, :],
                                                start=False, stop=(t == 2), skip_group_check=True)
                    if m % 2:
                        last.then_inc([wide0_full, wide1_full][m // 2], 1)

            def do_layer2(c):
                bank = ring_bank(("layer2", c))
                if c == 0:
                    pe.wait_ge(w2_loaded, 16)
                for k in range(H1 // P):
                    if k == 0:
                        pe.wait_ge(hid1_act, c + 1)
                    if k == 2:
                        pe.wait_ge(hid1_dve, c + 1)
                    for m in range(H2 // P):
                        last = nc.tensor.matmul(bank[:, m * P:(m + 1) * P], w2s[:, k, m * P:(m + 1) * P],
                                                hid1[:, c % 2, k, :], start=(k == 0 and m == 0),
                                                stop=(k == H1 // P - 1), skip_group_check=True)
                last.then_inc(ring_full, 1)

            def do_layer3(c):
                bank = ring_bank(("layer3", c))
                if c == 0:
                    pe.wait_ge(small_loaded, 48)
                wait_ring_out(pe, RING[("layer2", c)])
                for k in range(H2 // P):
                    last = nc.tensor.matmul(bank[0:1, 0:P], w3s[:, k:k + 1], hid2[:, c % 2, k, :],
                                            start=(k == 0), stop=(k == H2 // P - 1))
                last.then_inc(ring_full, 1)

            steps = {"dense": do_dense, "turn": do_turn, "lookup": do_lookup, "gram": do_gram,
                     "pairs": do_pairs, "dense1": do_dense1, "layer1": do_layer1, "layer2": do_layer2, "layer3": do_layer3}
            pe.wait_ge(idle_zero, 1)
            for _ in range(WARM):
                nc.tensor.matmul(wide[1][:], idle[:, 0:P], idle[:], start=True, stop=True)
            for kind, *at in ORDER:
                if kind in steps:
                    steps[kind](*at)

        def feat_slots(c, g):
            return featT[:, c * P:(c + 1) * P, GROUP_AT[g]:GROUP_AT[g + 1]].rearrange("p b j -> p j b")

        def turned(bank, g):
            return bank[:, 0:(GROUP_AT[g + 1] - GROUP_AT[g]) * P].rearrange("p (j b) -> p j b", b=P)

        @block.scalar
        def _(act):
            def split_high(q):
                act.wait_ge(table_loaded[q], 32)
                if q >= 2:
                    act.wait_ge(hot_used, KL * (q - 1))
                for ks in steps_of(q):
                    nc.scalar.activation(high[0:RP, q % 2, ks], table[0:RP, q % 2, ks], ACT.Copy).then_inc(high_ready, 1)

            def make_hot(q):
                if q == 0:
                    act.wait_ge(rowid_loaded, 16)
                act.wait_ge(want_loaded[q], 16)
                if q:
                    act.wait_ge(hot_act, q * (KL - KV))
                for k in range(KV, KL):
                    nc.scalar.activation(apart[0:RP, k - KV], want[0:RP, q, :], ACT.Abs, bias=rowid[0:RP, k:k + 1],
                                         scale=-1.0).then_inc(apart_done, 1)
                for k in range(KV, KL):
                    n = q * KL + k
                    if n >= HOT:
                        act.wait_ge(hot_used, n - HOT + 1)
                    act.wait_ge(apart_done, q * (KL - KV) + k - KV + 1)
                    nc.scalar.activation(hot[0:RP, n % HOT, :], apart[0:RP, k - KV], ACT.Relu, bias=1.0, scale=-1.0
                                         ).then_inc(hot_act, 1)

            split_high(0)
            make_hot(0)
            for s in ORDER:
                kind, at = s[0], s[1:]
                if kind == "lookup":
                    q, = at
                    if q + 1 < NL:
                        split_high(q + 1)
                        make_hot(q + 1)
                    act.wait_ge(hot_used, KL * (q + 1))
                    nc.scalar.activation(featT[:, :, NG + q], wide[q % 2][:], ACT.Copy).then_inc(looked_up, 1)
                elif kind == "gram":
                    c, h = at
                    n = c * PARTS + h
                    act.wait_ge(gram_full, n + 1)
                    if c >= 2 and h == 0:
                        act.wait_ge(flip_done, c - 1)
                    for s4 in range(2):
                        part = slice(s4 * QS, (s4 + 1) * QS)
                        last = nc.scalar.activation(gram_rows[part, c % 2, h * MM:(h + 1) * MM, :],
                                                    gram[n % 2][part, :, s4 * NJ:(s4 + 1) * NJ], ACT.Copy)
                    last.then_inc(gram_act, 1)
                elif kind == "layer1":
                    c, = at
                    if c == 0:
                        act.wait_ge(small_loaded, 48)
                    act.wait_ge(wide0_full, c + 1)
                    if c >= 2:
                        act.wait_ge(ring_full, RING[("layer2", c - 2)] + 1)
                    for m in range(2):
                        last = nc.scalar.activation(hid1[:, c % 2, m, :], wide[0][:, m * P:(m + 1) * P],
                                                    ACT.Relu, bias=b1s[:, m:m + 1])
                    last.then_inc(hid1_act, 1)
                elif s in RING and RING[s] % 2:
                    n = RING[s]
                    bank = ring[1]
                    act.wait_ge(ring_full, n + 1)
                    if kind == "turn":
                        nc.scalar.activation(feat_slots(*at), turned(bank, at[1]),
                                             ACT.Copy).then_inc(ring_act, 1)
                    elif kind == "pairs":
                        c, = at
                        if c >= 2:
                            act.wait_ge(wide1_full, c - 1)
                        nc.scalar.activation(interT[0:KZ, c % 2], bank[0:KZ, 0:3 * P].rearrange("p (t b) -> p t b", b=P),
                                             ACT.Copy).then_inc(ring_act, 1)
                    elif kind == "layer2":
                        c, = at
                        if c >= 2:
                            act.wait_ge(ring_full, RING[("layer3", c - 2)] + 1)
                        for m in range(H2 // P):
                            last = nc.scalar.activation(hid2[:, c % 2, m, :], bank[:, m * P:(m + 1) * P],
                                                        ACT.Relu, bias=b2s[:, m:m + 1])
                        last.then_inc(ring_act, 1)
                    elif kind == "layer3":
                        c, = at
                        nc.scalar.activation(y[0:1, c * P:(c + 1) * P].rearrange("o (g s) -> o s g", s=4),
                                             bank[0:1, 0:P].rearrange("o (s g) -> o s g", s=4),
                                             ACT.Copy).then_inc(ring_act, 1)

        @block.vector
        def _(dve):
            def make_hot(q):
                if q == 0:
                    dve.wait_ge(rowid_loaded, 16)
                dve.wait_ge(want_loaded[q], 16)
                for k in range(KV):
                    n = q * KL + k
                    if n >= HOT:
                        dve.wait_ge(hot_used, n - HOT + 1)
                    nc.vector.tensor_scalar(hot[0:RP, n % HOT, :], want[0:RP, q, :], rowid[0:RP, k:k + 1], None,
                                            ALU.is_equal).then_inc(hot_dve, 1)
                    if k == 1:
                        split_low(q)

            def split_low(q):
                if q >= 2:
                    dve.wait_ge(hot_used, KL * (q - 1))
                for n, ks in enumerate(steps_of(q)):
                    dve.wait_ge(high_ready, halves(q) - len(steps_of(q)) + n + 1)
                    nc.vector.tensor_tensor(low[0:RP, q % 2, ks], table[0:RP, q % 2, ks],
                                            high[0:RP, q % 2, ks].bitcast(f32), ALU.subtract).then_inc(low_ready, 1)

            nc.vector.memset(idle[:], 0.0).then_inc(idle_zero, 1)
            make_hot(0)
            for s in ORDER:
                kind, at = s[0], s[1:]
                if kind == "dense":
                    assert RING[s] % 2 == 0
                    dve.wait_ge(ring_full, RING[s] + 1)
                    nc.vector.tensor_copy(featT[:, :, DENSE], ring[0][:])
                    nc.vector.tensor_copy(denseT[:], ring[0][:].rearrange("p (c g s) -> p c s g", c=CHUNKS, s=4)
                                          ).then_inc(ring_dve, 1)
                elif kind == "lookup":
                    q, = at
                    if q + 1 < NL:
                        make_hot(q + 1)
                    if q == NL - 1:
                        nc.vector.memset(featT[:, :, DENSE + 1:SLOTS], 0.0).then_inc(pads_zero, 1)
                        dve.wait_ge(wd_loaded, 16)
                        nc.vector.tensor_tensor(wds[:], wd[:, 0, :], wd[:, 1, :], ALU.add).then_inc(wds_ready, 1)
                elif kind == "gram":
                    c, h = at
                    n = c * PARTS + h
                    dve.wait_ge(gram_full, n + 1)
                    if c >= 2 and h == 0:
                        dve.wait_ge(flip_done, c - 1)
                    for s4 in range(2, 4):
                        part = slice(s4 * QS, (s4 + 1) * QS)
                        last = nc.vector.tensor_copy(gram_rows[part, c % 2, h * MM:(h + 1) * MM, :],
                                                     gram[n % 2][part, :, s4 * NJ:(s4 + 1) * NJ])
                    last.then_inc(gram_dve, 1)
                elif kind == "flip":
                    c, = at
                    dve.wait_ge(gram_act, PARTS * (c + 1))
                    dve.wait_ge(gram_dve, PARTS * (c + 1))
                    if c >= 1:
                        dve.wait_ge(inter_ready, c)
                    nc.vector.transpose(flipped[:, :, 0:SLOTS], gram_rows[:, c % 2].rearrange("p g j -> p j g")
                                        ).then_inc(flip_done, 1)
                    dve.wait_ge(flip_done, c + 1)
                    flat = flipped[:].rearrange("p j i -> p (j i)")
                    first = (F - 2) * FOLDW + F - 1
                    fold_out = flat[:, first:first + 1]
                    fold_out = bass.AP(tensor=fold_out.tensor, offset=fold_out.offset,
                                       ap=[list(fold_out.ap[0]), [-(FOLDW + 1), FOLD], [1, FOLD]])
                    nc.vector.tensor_copy(fold_out, flipped[:, 0:FOLD, 0:FOLD]).then_inc(fold_done, 1)
                    dve.wait_ge(fold_done, c + 1)
                    if c >= 2:
                        dve.wait_ge(ring_full, RING[("pairs", c - 2)] + 1)
                    lo = NJ - ZROWS
                    nc.vector.tensor_copy(inter[:, c % 2], flipped[:, NJ - 1:lo - 1:-1, 0:F]).then_inc(inter_ready, 1)
                elif kind == "layer1":
                    c, = at
                    if c == 0:
                        dve.wait_ge(small_loaded, 48)
                    dve.wait_ge(wide1_full, c + 1)
                    if c >= 2:
                        dve.wait_ge(ring_full, RING[("layer2", c - 2)] + 1)
                    for m in range(2, 4):
                        last = nc.vector.tensor_scalar(hid1[:, c % 2, m, :], wide[1][:, (m - 2) * P:(m - 1) * P],
                                                       b1s[:, m:m + 1], 0.0, ALU.add, ALU.max)
                    last.then_inc(hid1_dve, 1)
                elif s in RING and RING[s] % 2 == 0:
                    n = RING[s]
                    bank = ring[0]
                    dve.wait_ge(ring_full, n + 1)
                    if kind == "turn":
                        nc.vector.tensor_copy(feat_slots(*at), turned(bank, at[1])
                                              ).then_inc(ring_dve, 1)
                    elif kind == "pairs":
                        c, = at
                        if c >= 2:
                            dve.wait_ge(wide1_full, c - 1)
                        nc.vector.tensor_copy(interT[0:KZ, c % 2], bank[0:KZ, 0:3 * P].rearrange("p (t b) -> p t b", b=P)
                                              ).then_inc(ring_dve, 1)
                    elif kind == "layer2":
                        c, = at
                        if c >= 2:
                            dve.wait_ge(ring_full, RING[("layer3", c - 2)] + 1)
                        for m in range(H2 // P):
                            last = nc.vector.tensor_scalar(hid2[:, c % 2, m, :], bank[:, m * P:(m + 1) * P],
                                                           b2s[:, m:m + 1], 0.0, ALU.add, ALU.max)
                        last.then_inc(ring_dve, 1)
                    elif kind == "layer3":
                        c, = at
                        nc.vector.tensor_copy(y[0:1, c * P:(c + 1) * P].rearrange("o (g s) -> o s g", s=4),
                                              bank[0:1, 0:P].rearrange("o (s g) -> o s g", s=4)).then_inc(ring_dve, 1)


def kernel(**inputs):
    import numpy as np
    import concourse.bacc as bacc
    from concourse.bass_utils import run_bass_kernel_spmd

    ids = np.asarray(inputs["ids"])
    w1 = np.asarray(inputs["W_top1"])
    arrays = {
        "ids_gather": ids[:, GATHER].reshape(CHUNKS, P, NG).transpose(1, 0, 2),
        "ids_lookup": ids[:, LOOKUP].T[None],
        "row_ids": np.pad(np.arange(LROWS, dtype=np.float32).reshape(RP, KL), ((0, P - RP), (0, 0)), constant_values=-1),
        "identity": np.eye(P, dtype=np.float32),
        "dense": inputs["r_dense_features"],
        "w_pairs": w1[interaction_rows()].reshape(3, KZ, H1).transpose(1, 0, 2),
        "w_dense": np.stack([w1[0:D], w1[D + NZ:]], axis=1),
        "w2": inputs["W_top2"],
        "w3": np.asarray(inputs["W_top3"]).reshape(H2 // P, P).T,
        "b1": np.asarray(inputs["b_top1"]).reshape(H1 // P, P).T,
        "b2": np.asarray(inputs["b_top2"]).reshape(H2 // P, P).T,
    }
    for f in range(F):
        arrays[f"tbl_{f}"] = inputs[f"tbl_{f}"]
    arrays = {name: np.ascontiguousarray(a) for name, a in arrays.items()}

    nc = bacc.Bacc("TRN2", target_bir_lowering=False, num_devices=1)
    aps = {name: nc.dram_tensor(name, a.shape, mybir.dt.from_np(a.dtype), kind="ExternalInput").ap()
           for name, a in arrays.items()}
    out = nc.dram_tensor("out", (1, B), mybir.dt.float32, kind="ExternalOutput").ap()
    build(nc, aps["ids_gather"], aps["ids_lookup"].to_broadcast([P, NL, B]), aps["row_ids"], aps["identity"], aps["dense"],
          [aps[f"tbl_{f}"] for f in range(F)], aps["w_pairs"], aps["w_dense"], aps["w2"], aps["w3"],
          aps["b1"], aps["b2"], out)
    r = run_bass_kernel_spmd(nc, [arrays], core_ids=[0])
    return r.results[0]["out"].reshape(B, 1)
```

```python
import concourse.bass as bass
from concourse import mybir
from contextlib import ExitStack

P = 128
B = 512
D = 128
F = 26
H1, H2 = 512, 256
CHUNKS = B // P
LOOKUP = [3, 4, 7, 8, 11, 19, 20, 21]
LROWS = 1000
KL = 8
RP = LROWS // KL
GATHER = [f for f in range(F) if f not in LOOKUP]
SLOT_FIELDS = GATHER + LOOKUP
NG, NL = len(GATHER), len(LOOKUP)
DENSE = F
ROWSM = 3 * 32 + F
SLOTS = 32
GROUPS = -(-NG // 4)
GROUP_AT = [NG - NG * (GROUPS - g) // GROUPS for g in range(GROUPS + 1)]
GROUP_OF = [g for g in range(GROUPS) for _ in range(GROUP_AT[g], GROUP_AT[g + 1])]
NJ = F
QS = 32
MM = 4
PARTS = QS // MM
FOLDW = 40
FOLD = 12
ZROWS = 14
NPAIR = F * (F - 1) // 2
NZ = F + NPAIR
WARM = 12
KZ = NZ // 3
ROWBUFS = 3
HOT = 12
KV = 6


def interaction_rows():
    pair_row, n = {}, D + F
    for i in range(F):
        for j in range(i + 1, F):
            pair_row[i, j] = n
            n += 1
    rows = []
    for r in range(ZROWS):
        for c in range(F):
            j = F - r
            if r == 0:
                rows.append(D + SLOT_FIELDS[c])
            elif c < j:
                a, b = SLOT_FIELDS[c], SLOT_FIELDS[j]
                rows.append(pair_row[min(a, b), max(a, b)])
            elif r <= FOLD:
                a, b = SLOT_FIELDS[c - j], SLOT_FIELDS[r]
                rows.append(pair_row[min(a, b), max(a, b)])
    return rows


def schedule():
    cost = {"lookup": 3.5, "gram": 0.8, "pairs": 0.3, "dense1": 0.9, "layer1": 2.6, "layer2": 0.9, "layer3": 0.4}
    turns = [("turn", c, g) for c in range(CHUNKS) for g in range(GROUPS)]
    order, clock, done = [], 7.0, 0

    def ready(n):
        return 5.0 + 1.04 * (n // GROUPS * NG + GROUP_AT[n % GROUPS + 1])

    def grams(c, a, b):
        return [("gram", c, h) for h in range(a, b)] + [("flip", c)] * (b == PARTS)

    def layer2(c):
        return [("layer2", c, m) for m in range(H2 // P)]

    main = [("lookup", q) for q in range(NL - 1)] + [("dense",), ("lookup", NL - 1)]
    main += grams(0, 0, PARTS) + grams(1, 0, PARTS // 2) + [("dense1", 0), ("pairs", 0)] + grams(1, PARTS // 2, PARTS)
    main += [("layer1", 0), ("pairs", 1), *layer2(0), ("dense1", 1), ("layer3", 0), ("layer1", 1)]
    main += grams(2, 0, PARTS)
    main += [*layer2(1), ("dense1", 2), ("pairs", 2), ("layer3", 1), ("layer1", 2), ("dense1", 3)]
    main += grams(3, 0, PARTS)
    main += [*layer2(2), ("pairs", 3), ("layer3", 2), ("layer1", 3), *layer2(3), ("layer3", 3)]
    needed = {("gram", 1, 0): 2 * GROUPS}
    needed |= {("layer1", 1): 3 * GROUPS, ("dense1", 3): 4 * GROUPS}
    for s in main:
        kept = 1 if s in (("dense",), ("lookup", NL - 1)) else 0
        here = 0
        if s == ("gram", 0, 0):
            clock += 1
        while s[0] != "layer2" and done < len(turns) and (done < needed.get(s, 0) or (done + kept < len(turns)
                                     and ready(done + kept) <= clock and here < 2)):
            clock = max(clock, ready(done)) + 0.4
            order.append(turns[done])
            done += 1
            here += 1
        order.append(s)
        clock += cost.get(s[0], 0)
    return order


ORDER = schedule()
RING = {}
RBANKS = GBANKS = 3
for _s in ORDER:
    if _s[0] in ("dense", "turn", "pairs", "layer2", "layer3"):
        RING[_s] = len(RING)


def build(nc, ids_gather, ids_lookup, row_ids, identity, dense, tables, w_pairs, w_dense, w2, w3, b1, b2, out):
    f32, f32r, i32 = mybir.dt.float32, mybir.dt.float32r, mybir.dt.int32
    ALU = mybir.AluOpType
    ACT = mybir.ActivationFunctionType

    with ExitStack() as ctx:
        def sb(name, shape, dt=f32):
            return ctx.enter_context(nc.sbuf_tensor(name, shape, dt))

        def pb(name, shape):
            return ctx.enter_context(nc.psum_tensor(name, shape, f32))

        def sem(name):
            return ctx.enter_context(nc.semaphore(name))

        featT = sb("featT", [P, B, SLOTS])
        rows = sb("rows", [P, ROWBUFS, NG, D])
        idx = sb("idx", [P, CHUNKS, NG], i32)
        want = sb("want", [P, NL, B], i32)
        rowid = sb("rowid", [P, KL])
        ident = sb("ident", [P, P])
        dense_rows = sb("dense_rows", [P, CHUNKS, D])
        denseT = sb("denseT", [P, CHUNKS, 4, QS])
        table = sb("table", [P, 2, KL, D])
        high = sb("high", [P, 2, KL, D], f32r)
        low = sb("low", [P, 2, KL, D], f32r)
        hot = sb("hot", [P, HOT, B], f32r)
        apart = sb("apart", [P, KL - KV, B])
        wp = sb("wp", [P, 3, H1])
        wd = sb("wd", [P, 2, H1])
        wds = sb("wds", [P, H1])
        w2s = sb("w2s", [P, H1 // P, H2])
        w3s = sb("w3s", [P, H2 // P])
        b1s = sb("b1s", [P, H1 // P])
        b2s = sb("b2s", [P, H2 // P])
        gram_rows = sb("gram_rows", [P, 2, QS, NJ])
        flipped = sb("flipped", [P, NJ, FOLDW])
        inter = sb("inter", [P, 2, ZROWS, F])
        interT = sb("interT", [P, 2, 3, P])
        hid1 = sb("hid1", [P, 2, H1 // P, P])
        hid2 = sb("hid2", [P, 2, H2 // P, P])
        y = sb("y", [1, B])
        idle = sb("idle", [P, B], mybir.dt.bfloat16)

        ring = [pb(f"ring{i}", [P, 512]) for i in range(RBANKS)]
        gram = [pb(f"gram{i}", [P, MM, P]) for i in range(GBANKS)]
        wide = [pb(f"wide{i}", [P, 512]) for i in range(2)]

        idx_loaded = sem("idx_loaded")
        want_loaded = [sem(f"want_loaded{q}") for q in range(NL)]
        rowid_loaded = sem("rowid_loaded")
        ident_loaded = sem("ident_loaded")
        dense_loaded = sem("dense_loaded")
        table_loaded = [sem(f"table_loaded{q}") for q in range(NL)]
        wp_loaded = sem("wp_loaded")
        wd_loaded = sem("wd_loaded")
        w2_loaded = sem("w2_loaded")
        small_loaded = sem("small_loaded")
        gathered = [[sem(f"gathered{c}_{g}") for g in range(GROUPS)] for c in range(CHUNKS)]
        idle_zero = sem("idle_zero")
        gram_rows_zero = sem("gram_rows_zero")
        pads_zero = sem("pads_zero")
        wds_ready = sem("wds_ready")
        hot_dve = sem("hot_dve")
        hot_act = sem("hot_act")
        apart_done = sem("apart_done")
        high_ready = sem("high_ready")
        low_ready = sem("low_ready")
        hot_used = sem("hot_used")
        looked_up = sem("looked_up")
        ring_full = sem("ring_full")
        ring_dve = sem("ring_dve")
        ring_act = sem("ring_act")
        gram_full = sem("gram_full")
        gram_dve = sem("gram_dve")
        gram_act = sem("gram_act")
        flip_done = sem("flip_done")
        fold_done = sem("fold_done")
        inter_ready = sem("inter_ready")
        wide0_full = sem("wide0_full")
        wide1_full = sem("wide1_full")
        hid1_act = sem("hid1_act")
        hid1_dve = sem("hid1_dve")
        stored = sem("stored")
        block = ctx.enter_context(nc.Block())

        last_chunk_entry = {c: RING[("turn", c, GROUPS - 1)] for c in range(CHUNKS)}

        def wait_ring_out(eng, n):
            eng.wait_ge(ring_act if n % 2 else ring_dve, n // 2 + 1)

        def halves(q):
            return q + 2

        def steps_of(q):
            return [slice(0, KL // 2), slice(KL // 2, KL)] if q == 0 else [slice(0, KL)]

        @block.sync
        def _(sp):
            sp.dma_start(idx[:], ids_gather).then_inc(idx_loaded, 16)

            def load_table(q):
                if q >= 2:
                    sp.wait_ge(high_ready, halves(q - 2))
                    sp.wait_ge(low_ready, halves(q - 2))
                src = tables[SLOT_FIELDS[NG + q]].rearrange("(p k) d -> p k d", k=KL)
                sp.dma_start(table[0:112, q % 2], src[0:112]).then_inc(table_loaded[q], 16)
                if q == 0:
                    sp.dma_start(rowid[:], row_ids).then_inc(rowid_loaded, 16)
                sp.dma_start(table[112:RP, q % 2], src[112:RP]).then_inc(table_loaded[q], 16)
                sp.dma_start(want[:, q, :], ids_lookup[:, q, :]).then_inc(want_loaded[q], 16)

            load_table(0)
            load_table(1)
            sp.dma_start(ident[:], identity).then_inc(ident_loaded, 16)
            sp.dma_start(dense_rows[:], dense.rearrange("(c p) d -> p c d", p=P)).then_inc(dense_loaded, 16)
            w2_rows = w2.rearrange("(k p) n -> p k n", p=P)
            weights = [(wp[0:KZ, t], w_pairs[:, t], wp_loaded) for t in range(3)]
            weights += [(wd[:, t], w_dense[:, t], wd_loaded) for t in range(2)]
            weights += [(w2s[:, 2 * t:2 * t + 2], w2_rows[:, 2 * t:2 * t + 2], w2_loaded) for t in range(2)]
            weights += [(w3s[:], w3, small_loaded), (b1s[:], b1, small_loaded), (b2s[:], b2, small_loaded)]
            for q in range(2, NL):
                load_table(q)
                for to, what, loaded in weights[q - 2::NL - 2]:
                    sp.dma_start(to, what).then_inc(loaded, 16)
            wait_ring_out(sp, RING[("layer3", CHUNKS - 1)])
            wait_ring_out(sp, RING[("layer3", CHUNKS - 2)])
            sp.dma_start(out, y[:]).then_inc(stored, 16)
            sp.wait_ge(stored, 16)

        @block.gpsimd
        def _(pool):
            nc.gpsimd.memset(gram_rows[:], 0.0).then_inc(gram_rows_zero, 1)
            pool.wait_ge(idx_loaded, 16)
            for c in range(CHUNKS):
                for f in range(NG):
                    if c >= ROWBUFS and f in GROUP_AT:
                        pool.wait_ge(ring_full, RING[("turn", c - ROWBUFS, GROUP_OF[f])] + 1)
                    pool.indirect_dma_start(
                        rows[:, c % ROWBUFS, f, :], None, tables[GATHER[f]],
                        bass.IndirectOffsetOnAxis(ap=idx[:, c, f:f + 1], axis=0),
                    ).then_inc(gathered[c][GROUP_OF[f]], 16)

        @block.tensor
        def _(pe):
            def ring_bank(s):
                n = RING[s]
                if n >= RBANKS:
                    wait_ring_out(pe, n - RBANKS)
                return ring[n % RBANKS]

            def do_dense():
                pe.wait_ge(ident_loaded, 16)
                pe.wait_ge(dense_loaded, 16)
                bank = ring_bank(("dense",))
                for c in range(CHUNKS):
                    last = nc.tensor.transpose(bank[:, c * P:(c + 1) * P], dense_rows[:, c, :], ident[:])
                last.then_inc(ring_full, 1)

            def do_turn(c, g):
                bank = ring_bank(("turn", c, g))
                if (c, g) == (0, 0):
                    pe.wait_ge(ident_loaded, 16)
                pe.wait_ge(gathered[c][g], 16 * (GROUP_AT[g + 1] - GROUP_AT[g]))
                for e, f in enumerate(range(GROUP_AT[g], GROUP_AT[g + 1])):
                    last = nc.tensor.transpose(bank[:, e * P:(e + 1) * P], rows[:, c % ROWBUFS, f, :], ident[:])
                last.then_inc(ring_full, 1)

            def do_lookup(q):
                if q >= 2:
                    pe.wait_ge(looked_up, q - 1)
                for k in range(KL):
                    if k == 0 or (q == 0 and k == KL // 2):
                        ready = halves(q) - (q == 0 and k == 0)
                        pe.wait_ge(high_ready, ready)
                        pe.wait_ge(low_ready, ready)
                    if k < KV:
                        pe.wait_ge(hot_dve, q * KV + k + 1)
                    else:
                        pe.wait_ge(hot_act, q * (KL - KV) + k - KV + 1)
                    mov = hot[0:RP, (q * KL + k) % HOT, :]
                    nc.tensor.matmul(wide[q % 2][:], high[0:RP, q % 2, k, :], mov, start=(k == 0), stop=False)
                    nc.tensor.matmul(wide[q % 2][:], low[0:RP, q % 2, k, :], mov, start=False,
                                     stop=(k == KL - 1)).then_inc(hot_used, 1)

            def do_gram(c, h):
                n = c * PARTS + h
                if h == 0:
                    wait_ring_out(pe, last_chunk_entry[c])
                    wait_ring_out(pe, last_chunk_entry[c] - 1)
                    if c == 0:
                        wait_ring_out(pe, RING[("dense",)])
                        pe.wait_ge(looked_up, NL)
                        pe.wait_ge(pads_zero, 1)
                if n >= GBANKS:
                    pe.wait_ge(gram_dve, n - GBANKS + 1)
                    pe.wait_ge(gram_act, n - GBANKS + 1)
                for m in range(MM):
                    s = c * P + 4 * (h * MM + m)
                    last = nc.tensor.matmul(gram[n % GBANKS][0:ROWSM, m, 0:4 * NJ],
                                            featT[:, s:s + 4, :].rearrange("p s j -> p (s j)")[:, 0:ROWSM],
                                            featT[:, s:s + 4, 1:1 + NJ], start=True, stop=True)
                last.then_inc(gram_full, 1)

            def do_pairs(c):
                bank = ring_bank(("pairs", c))
                pe.wait_ge(inter_ready, c + 1)
                z = inter[:, c % 2].rearrange("p r j -> p (r j)")
                for t in range(3):
                    last = nc.tensor.transpose(bank[0:KZ, t * P:(t + 1) * P], z[:, t * KZ:(t + 1) * KZ], ident[:])
                last.then_inc(ring_full, 1)

            def do_dense1(c):
                if c == 0:
                    pe.wait_ge(wds_ready, 1)
                    pe.wait_ge(looked_up, NL)
                for m in range(H1 // P):
                    if c >= 1 and m == 0:
                        pe.wait_ge(hid1_act, c)
                    if c >= 1 and m == 2:
                        pe.wait_ge(hid1_dve, c)
                    nc.tensor.matmul(wide[m // 2][:, (m % 2) * P:(m % 2 + 1) * P], wds[:, m * P:(m + 1) * P],
                                     denseT[:, c].rearrange("p s g -> p (s g)"),
                                     start=(m % 2 == 0), stop=False, skip_group_check=True)

            def do_layer1(c):
                if c == 0:
                    pe.wait_ge(wp_loaded, 48)
                wait_ring_out(pe, RING[("pairs", c)])
                for m in range(H1 // P):
                    for t in range(3):
                        last = nc.tensor.matmul(wide[m // 2][:, (m % 2) * P:(m % 2 + 1) * P],
                                                wp[0:KZ, t, m * P:(m + 1) * P], interT[0:KZ, c % 2, t, :],
                                                start=False, stop=(t == 2), skip_group_check=True)
                    if m % 2:
                        last.then_inc([wide0_full, wide1_full][m // 2], 1)

            def do_layer2(c, half):
                if half:
                    return
                banks = [ring_bank(("layer2", c, m)) for m in range(H2 // P)]
                if c == 0:
                    pe.wait_ge(w2_loaded, 32)
                for k in range(H1 // P):
                    if k == 0:
                        pe.wait_ge(hid1_act, c + 1)
                    if k == 2:
                        pe.wait_ge(hid1_dve, c + 1)
                    for m in range(H2 // P):
                        last = nc.tensor.matmul(banks[m][:, 0:P], w2s[:, k, m * P:(m + 1) * P], hid1[:, c % 2, k, :],
                                                start=(k == 0), stop=(k == H1 // P - 1))
                        if k == H1 // P - 1:
                            last.then_inc(ring_full, 1)

            def do_layer3(c):
                bank = ring_bank(("layer3", c))
                if c == 0:
                    pe.wait_ge(small_loaded, 48)
                for k in range(H2 // P):
                    wait_ring_out(pe, RING[("layer2", c, k)])
                    last = nc.tensor.matmul(bank[0:1, 0:P], w3s[:, k:k + 1], hid2[:, c % 2, k, :],
                                            start=(k == 0), stop=(k == H2 // P - 1))
                last.then_inc(ring_full, 1)

            sections = {"dense": do_dense, "turn": do_turn, "lookup": do_lookup, "gram": do_gram, "pairs": do_pairs,
                        "dense1": do_dense1, "layer1": do_layer1, "layer2": do_layer2, "layer3": do_layer3}
            pe.wait_ge(idle_zero, 1)
            for _ in range(WARM):
                nc.tensor.matmul(wide[1][:], idle[:, 0:P], idle[:], start=True, stop=True)
            for kind, *at in ORDER:
                if kind in sections:
                    sections[kind](*at)

        def feat_slots(c, g):
            return featT[:, c * P:(c + 1) * P, GROUP_AT[g]:GROUP_AT[g + 1]].rearrange("p b j -> p j b")

        def turned(bank, g):
            return bank[:, 0:(GROUP_AT[g + 1] - GROUP_AT[g]) * P].rearrange("p (j b) -> p j b", b=P)

        def by_remainder(bank):
            return bank[:].rearrange("p (c g s) -> p c s g", c=CHUNKS, s=4)

        @block.scalar
        def _(act):
            def split_high(q):
                act.wait_ge(table_loaded[q], 32)
                if q >= 2:
                    act.wait_ge(hot_used, KL * (q - 1))
                for ks in steps_of(q):
                    nc.scalar.activation(high[0:RP, q % 2, ks], table[0:RP, q % 2, ks], ACT.Copy).then_inc(high_ready, 1)

            def make_hot(q):
                if q == 0:
                    act.wait_ge(rowid_loaded, 16)
                act.wait_ge(want_loaded[q], 16)
                if q:
                    act.wait_ge(hot_act, q * (KL - KV))
                for k in range(KV, KL):
                    nc.scalar.activation(apart[0:RP, k - KV], want[0:RP, q, :], ACT.Abs, bias=rowid[0:RP, k:k + 1],
                                         scale=-1.0).then_inc(apart_done, 1)
                for k in range(KV, KL):
                    n = q * KL + k
                    if n >= HOT:
                        act.wait_ge(hot_used, n - HOT + 1)
                    act.wait_ge(apart_done, q * (KL - KV) + k - KV + 1)
                    nc.scalar.activation(hot[0:RP, n % HOT, :], apart[0:RP, k - KV], ACT.Relu, bias=1.0, scale=-1.0
                                         ).then_inc(hot_act, 1)

            split_high(0)
            make_hot(0)
            for s in ORDER:
                kind, at = s[0], s[1:]
                if kind == "lookup":
                    q, = at
                    if q + 1 < NL:
                        split_high(q + 1)
                        make_hot(q + 1)
                    act.wait_ge(hot_used, KL * (q + 1))
                    nc.scalar.activation(featT[:, :, NG + q], wide[q % 2][:], ACT.Copy).then_inc(looked_up, 1)
                elif kind == "gram":
                    c, h = at
                    n = c * PARTS + h
                    act.wait_ge(gram_full, n + 1)
                    if n == 0:
                        act.wait_ge(gram_rows_zero, 1)
                    if c >= 2 and h == 0:
                        act.wait_ge(flip_done, c - 1)
                    for s4 in range(2):
                        part = slice(s4 * QS, s4 * QS + F)
                        last = nc.scalar.activation(gram_rows[part, c % 2, h * MM:(h + 1) * MM, :],
                                                    gram[n % GBANKS][part, :, s4 * NJ:(s4 + 1) * NJ], ACT.Copy)
                    last.then_inc(gram_act, 1)
                elif kind == "layer1":
                    c, = at
                    if c == 0:
                        act.wait_ge(small_loaded, 48)
                    act.wait_ge(wide0_full, c + 1)
                    if c >= 2:
                        act.wait_ge(ring_full, RING[("layer2", c - 2, 1)] + 1)
                    for m in range(2):
                        last = nc.scalar.activation(hid1[:, c % 2, m, :], wide[0][:, m * P:(m + 1) * P],
                                                    ACT.Relu, bias=b1s[:, m:m + 1])
                    last.then_inc(hid1_act, 1)
                elif s in RING and RING[s] % 2:
                    n = RING[s]
                    bank = ring[n % RBANKS]
                    act.wait_ge(ring_full, n + 1)
                    if kind == "dense":
                        nc.scalar.activation(featT[:, :, DENSE], bank[:], ACT.Copy)
                        nc.scalar.activation(denseT[:], by_remainder(bank), ACT.Copy).then_inc(ring_act, 1)
                    elif kind == "turn":
                        nc.scalar.activation(feat_slots(*at), turned(bank, at[1]),
                                             ACT.Copy).then_inc(ring_act, 1)
                    elif kind == "pairs":
                        c, = at
                        if c >= 2:
                            act.wait_ge(wide1_full, c - 1)
                        nc.scalar.activation(interT[0:KZ, c % 2], bank[0:KZ, 0:3 * P].rearrange("p (t b) -> p t b", b=P),
                                             ACT.Copy).then_inc(ring_act, 1)
                    elif kind == "layer2":
                        c, m = at
                        if c >= 2:
                            act.wait_ge(ring_full, RING[("layer3", c - 2)] + 1)
                        nc.scalar.activation(hid2[:, c % 2, m, :], bank[:, 0:P], ACT.Relu, bias=b2s[:, m:m + 1]
                                             ).then_inc(ring_act, 1)
                    elif kind == "layer3":
                        c, = at
                        nc.scalar.activation(y[0:1, c * P:(c + 1) * P].rearrange("o (g s) -> o s g", s=4),
                                             bank[0:1, 0:P].rearrange("o (s g) -> o s g", s=4),
                                             ACT.Copy).then_inc(ring_act, 1)

        @block.vector
        def _(dve):
            def split_low(q, n):
                ks = steps_of(q)[n]
                if q >= 2:
                    dve.wait_ge(hot_used, KL * (q - 1))
                dve.wait_ge(high_ready, halves(q) - len(steps_of(q)) + n + 1)
                nc.vector.tensor_tensor(low[0:RP, q % 2, ks], table[0:RP, q % 2, ks],
                                        high[0:RP, q % 2, ks].bitcast(f32), ALU.subtract).then_inc(low_ready, 1)

            def make_hot(q):
                if q == 0:
                    split_low(0, 0)
                    dve.wait_ge(rowid_loaded, 16)
                dve.wait_ge(want_loaded[q], 16)
                for k in range(KV):
                    n = q * KL + k
                    if n >= HOT:
                        dve.wait_ge(hot_used, n - HOT + 1)
                    nc.vector.tensor_scalar(hot[0:RP, n % HOT, :], want[0:RP, q, :], rowid[0:RP, k:k + 1], None,
                                            ALU.is_equal).then_inc(hot_dve, 1)
                    if k == 1:
                        split_low(q, len(steps_of(q)) - 1)

            nc.vector.memset(idle[:], 0.0).then_inc(idle_zero, 1)
            nc.vector.memset(featT[:, :, DENSE + 1:SLOTS], 0.0).then_inc(pads_zero, 1)
            make_hot(0)
            for s in ORDER:
                kind, at = s[0], s[1:]
                if kind == "lookup":
                    q, = at
                    if q + 1 < NL:
                        make_hot(q + 1)
                elif kind == "gram":
                    c, h = at
                    n = c * PARTS + h
                    dve.wait_ge(gram_full, n + 1)
                    if n == 0:
                        dve.wait_ge(gram_rows_zero, 1)
                    if c >= 2 and h == 0:
                        dve.wait_ge(flip_done, c - 1)
                    for s4 in range(2, 4):
                        part = slice(s4 * QS, s4 * QS + F)
                        last = nc.vector.tensor_copy(gram_rows[part, c % 2, h * MM:(h + 1) * MM, :],
                                                     gram[n % GBANKS][part, :, s4 * NJ:(s4 + 1) * NJ])
                    last.then_inc(gram_dve, 1)
                    if n == 0:
                        dve.wait_ge(wd_loaded, 32)
                        nc.vector.tensor_tensor(wds[:], wd[:, 0, :], wd[:, 1, :], ALU.add).then_inc(wds_ready, 1)
                elif kind == "flip":
                    c, = at
                    dve.wait_ge(gram_act, PARTS * (c + 1))
                    dve.wait_ge(gram_dve, PARTS * (c + 1))
                    if c >= 1:
                        dve.wait_ge(inter_ready, c)
                    nc.vector.transpose(flipped[:, :, 0:SLOTS], gram_rows[:, c % 2].rearrange("p g j -> p j g")
                                        ).then_inc(flip_done, 1)
                    dve.wait_ge(flip_done, c + 1)
                    flat = flipped[:].rearrange("p j i -> p (j i)")
                    first = (F - 2) * FOLDW + F - 1
                    fold_out = flat[:, first:first + 1]
                    fold_out = bass.AP(tensor=fold_out.tensor, offset=fold_out.offset,
                                       ap=[list(fold_out.ap[0]), [-(FOLDW + 1), FOLD], [1, FOLD]])
                    nc.vector.tensor_copy(fold_out, flipped[:, 0:FOLD, 0:FOLD]).then_inc(fold_done, 1)
                    dve.wait_ge(fold_done, c + 1)
                    if c >= 2:
                        dve.wait_ge(ring_full, RING[("pairs", c - 2)] + 1)
                    lo = NJ - ZROWS
                    nc.vector.tensor_copy(inter[:, c % 2], flipped[:, NJ - 1:lo - 1:-1, 0:F]).then_inc(inter_ready, 1)
                elif kind == "layer1":
                    c, = at
                    if c == 0:
                        dve.wait_ge(small_loaded, 48)
                    dve.wait_ge(wide1_full, c + 1)
                    if c >= 2:
                        dve.wait_ge(ring_full, RING[("layer2", c - 2, 1)] + 1)
                    for m in range(2, 4):
                        last = nc.vector.tensor_scalar(hid1[:, c % 2, m, :], wide[1][:, (m - 2) * P:(m - 1) * P],
                                                       b1s[:, m:m + 1], 0.0, ALU.add, ALU.max)
                    last.then_inc(hid1_dve, 1)
                elif s in RING and RING[s] % 2 == 0:
                    n = RING[s]
                    bank = ring[n % RBANKS]
                    dve.wait_ge(ring_full, n + 1)
                    if kind == "dense":
                        nc.vector.tensor_copy(featT[:, :, DENSE], bank[:])
                        nc.vector.tensor_copy(denseT[:], by_remainder(bank)).then_inc(ring_dve, 1)
                    elif kind == "turn":
                        nc.vector.tensor_copy(feat_slots(*at), turned(bank, at[1])
                                              ).then_inc(ring_dve, 1)
                    elif kind == "pairs":
                        c, = at
                        if c >= 2:
                            dve.wait_ge(wide1_full, c - 1)
                        nc.vector.tensor_copy(interT[0:KZ, c % 2], bank[0:KZ, 0:3 * P].rearrange("p (t b) -> p t b", b=P)
                                              ).then_inc(ring_dve, 1)
                    elif kind == "layer2":
                        c, m = at
                        if c >= 2:
                            dve.wait_ge(ring_full, RING[("layer3", c - 2)] + 1)
                        nc.vector.tensor_scalar(hid2[:, c % 2, m, :], bank[:, 0:P], b2s[:, m:m + 1], 0.0,
                                                ALU.add, ALU.max).then_inc(ring_dve, 1)
                    elif kind == "layer3":
                        c, = at
                        nc.vector.tensor_copy(y[0:1, c * P:(c + 1) * P].rearrange("o (g s) -> o s g", s=4),
                                              bank[0:1, 0:P].rearrange("o (s g) -> o s g", s=4)).then_inc(ring_dve, 1)


def kernel(**inputs):
    import numpy as np
    import concourse.bacc as bacc
    from concourse.bass_utils import run_bass_kernel_spmd

    ids = np.asarray(inputs["ids"])
    w1 = np.asarray(inputs["W_top1"])
    arrays = {
        "ids_gather": ids[:, GATHER].reshape(CHUNKS, P, NG).transpose(1, 0, 2),
        "ids_lookup": ids[:, LOOKUP].T[None],
        "row_ids": np.pad(np.arange(LROWS, dtype=np.float32).reshape(RP, KL), ((0, P - RP), (0, 0)), constant_values=-1),
        "identity": np.eye(P, dtype=np.float32),
        "dense": inputs["r_dense_features"],
        "w_pairs": w1[interaction_rows()].reshape(3, KZ, H1).transpose(1, 0, 2),
        "w_dense": np.stack([w1[0:D], w1[D + NZ:]], axis=1),
        "w2": inputs["W_top2"],
        "w3": np.asarray(inputs["W_top3"]).reshape(H2 // P, P).T,
        "b1": np.asarray(inputs["b_top1"]).reshape(H1 // P, P).T,
        "b2": np.asarray(inputs["b_top2"]).reshape(H2 // P, P).T,
    }
    for f in range(F):
        arrays[f"tbl_{f}"] = inputs[f"tbl_{f}"]
    arrays = {name: np.ascontiguousarray(a) for name, a in arrays.items()}

    nc = bacc.Bacc("TRN2", target_bir_lowering=False, num_devices=1)
    aps = {name: nc.dram_tensor(name, a.shape, mybir.dt.from_np(a.dtype), kind="ExternalInput").ap()
           for name, a in arrays.items()}
    out = nc.dram_tensor("out", (1, B), mybir.dt.float32, kind="ExternalOutput").ap()
    build(nc, aps["ids_gather"], aps["ids_lookup"].to_broadcast([P, NL, B]), aps["row_ids"], aps["identity"], aps["dense"],
          [aps[f"tbl_{f}"] for f in range(F)], aps["w_pairs"], aps["w_dense"], aps["w2"], aps["w3"],
          aps["b1"], aps["b2"], out)
    r = run_bass_kernel_spmd(nc, [arrays], core_ids=[0])
    return r.results[0]["out"].reshape(B, 1)
```
